# Optimizing a Trainium2 kernel written in Bass

```python
import numpy as np
import jax
import jax.numpy as jnp

def _softmax(x, axis=-1):
    return jax.nn.softmax(x, axis=axis)

def _gelu(x):
    return jax.nn.gelu(x, approximate=True)

def _silu(x):
    return jax.nn.silu(x)

def _sigmoid(x):
    return jax.nn.sigmoid(x)

def _layernorm(x, axis=-1, eps=1e-05):
    m = jnp.mean(x, axis=axis, keepdims=True)
    v = jnp.var(x, axis=axis, keepdims=True)
    return (x - m) / jnp.sqrt(v + eps)

def _scatter_add(tgt, idx, src, axis=0):
    return tgt.at[idx].add(src)

def _segment_sum(src, seg, n):
    return jax.ops.segment_sum(src, seg, n)
kernel_name = 'mk_adj_preln_d4_adj_r2_a666d0'

def setup_inputs(seed: int=0):
    np.random.seed(seed)
    _w = jnp.asarray

    def _rec_inputs():
        import jax
        import jax.numpy as jnp
        _gk = jax.random.key(seed)
        x = -0.0005207 + 1.001 * jax.random.normal(jax.random.fold_in(_gk, 1), (4096, 128), jnp.float32)
        _a = jax.random.bernoulli(jax.random.fold_in(_gk, 2), 0.00195312, (4096, 4096))
        _a = jnp.logical_or(_a, jnp.swapaxes(_a, -1, -2))
        _a = jnp.logical_or(_a, jnp.eye(4096, dtype=bool))
        _af = _a.astype(jnp.float32)
        _af = _af * jax.random.uniform(jax.random.fold_in(_gk, 3), (4096, 4096), jnp.float32, 0.05, 1)
        adj = _af
        return (x, adj)
    x, adj = _rec_inputs()

    def _L0_gnn_setup():
        import jax, jax.numpy as jnp
        import numpy as np
        N = 8192
        F_IN = 128
        F_OUT = 128
        key = jax.random.key(seed)
        k1, k2, k3, k4 = jax.random.split(key, 4)
        features = jax.random.normal(k1, (N, F_IN), dtype=jnp.float32)
        adj = jax.random.uniform(k2, (N, N), dtype=jnp.float32)
        kernel = jax.random.normal(k3, (F_IN, F_OUT), dtype=jnp.float32) * 0.02
        bias = jax.random.normal(k4, (F_OUT,), dtype=jnp.float32) * 0.02
        return {'features': features, 'adj': adj, 'kernel': kernel, 'bias': bias}
    _L0_gnn_all = _L0_gnn_setup()
    _L0_gnn_in = {k: v for k, v in _L0_gnn_all.items() if k in ('kernel', 'bias')}
    del _L0_gnn_all

    def _L1_gnn_setup():
        import jax, jax.numpy as jnp
        import numpy as np
        N = 4096
        D = 128
        key = jax.random.key(seed)
        kx, ka, kw1, kw2 = jax.random.split(key, 4)
        x = jax.random.normal(kx, (N, D), dtype=jnp.float32)
        A = jax.random.uniform(ka, (N, N), dtype=jnp.float32)
        s = 0.05
        W1 = jax.random.normal(kw1, (D, D), dtype=jnp.float32) * s
        b1 = jnp.zeros((D,), dtype=jnp.float32)
        W2 = jax.random.normal(kw2, (D, D), dtype=jnp.float32) * s
        b2 = jnp.zeros((D,), dtype=jnp.float32)
        return {'x': x, 'A': A, 'W1': W1, 'b1': b1, 'W2': W2, 'b2': b2}
    _L1_gnn_all = _L1_gnn_setup()
    _L1_gnn_in = {k: v for k, v in _L1_gnn_all.items() if k in ('W1', 'b1', 'W2', 'b2')}
    del _L1_gnn_all

    def _L2_gnn_setup():
        import jax, jax.numpy as jnp
        import numpy as np
        N = 8192
        F_IN = 128
        F_OUT = 128
        K = 3
        key = jax.random.key(seed)
        k1, k2, k3 = jax.random.split(key, 3)
        x = jax.random.normal(k1, (N, F_IN), dtype=jnp.float32)
        L_tilde = jax.random.normal(k2, (N, N), dtype=jnp.float32) / jnp.sqrt(jnp.float32(N))
        weight = jax.random.normal(k3, (K, F_IN, F_OUT), dtype=jnp.float32) * (1.0 / np.sqrt(F_IN))
        bias = jnp.zeros((F_OUT,), dtype=jnp.float32)
        return {'x': x, 'L_tilde': L_tilde, 'weight': weight, 'bias': bias}
    _L2_gnn_all = _L2_gnn_setup()
    _L2_gnn_in = {k: v for k, v in _L2_gnn_all.items() if k in ('weight', 'bias')}
    del _L2_gnn_all

    def _L3_gnn_setup():
        import jax, jax.numpy as jnp
        import numpy as np
        N, D_IN, D_OUT = (4096, 128, 128)
        key = jax.random.key(seed)
        k1, k2, k3 = jax.random.split(key, 3)
        x = jax.random.normal(k1, (N, D_IN), dtype=jnp.float32)
        adjacency_matrix = jax.random.uniform(k2, (N, N), dtype=jnp.float32)
        weight = jax.random.normal(k3, (D_IN, D_OUT), dtype=jnp.float32) * (1.0 / np.sqrt(D_IN))
        return {'x': x, 'adjacency_matrix': adjacency_matrix, 'weight': weight}
    _L3_gnn_all = _L3_gnn_setup()
    _L3_gnn_in = {k: v for k, v in _L3_gnn_all.items() if k in ('weight',)}
    del _L3_gnn_all
    return {'x': x, 'adj': adj, 'L0_gnn_kernel': _L0_gnn_in['kernel'], 'L0_gnn_bias': _L0_gnn_in['bias'], 'L1_gnn_W1': _L1_gnn_in['W1'], 'L1_gnn_b1': _L1_gnn_in['b1'], 'L1_gnn_W2': _L1_gnn_in['W2'], 'L1_gnn_b2': _L1_gnn_in['b2'], 'L2_gnn_weight': _L2_gnn_in['weight'], 'L2_gnn_bias': _L2_gnn_in['bias'], 'L3_gnn_weight': _L3_gnn_in['weight']}

def reference(x, adj, L0_gnn_kernel, L0_gnn_bias, L1_gnn_W1, L1_gnn_b1, L1_gnn_W2, L1_gnn_b2, L2_gnn_weight, L2_gnn_bias, L3_gnn_weight):
    import jax
    import jax.numpy as jnp

    def _L0_gnn_ref(features, adj, kernel, bias):
        import jax, jax.numpy as jnp
        import numpy as np
        N = 8192
        F_IN = 128
        F_OUT = 128
        xw = features @ kernel
        out = adj @ xw
        return jax.nn.relu(out + bias)

    def _L1_gnn_ref(x, A, W1, b1, W2, b2):
        import jax, jax.numpy as jnp
        import numpy as np
        N = 4096
        D = 128
        h = jax.nn.relu(jnp.matmul(A, jnp.matmul(x, W1)) + b1)
        h = jax.nn.relu(jnp.matmul(A, jnp.matmul(h, W2)) + b2)
        return h

    def _L2_gnn_ref(x, L_tilde, weight, bias):
        import jax, jax.numpy as jnp
        import numpy as np
        N = 8192
        F_IN = 128
        F_OUT = 128
        K = 3
        T_prev = x
        T_curr = L_tilde @ x
        out = T_prev @ weight[0]
        if K > 1:
            out = out + T_curr @ weight[1]
        for k in range(2, K):
            T_next = 2.0 * (L_tilde @ T_curr) - T_prev
            out = out + T_next @ weight[k]
            T_prev, T_curr = (T_curr, T_next)
        return out + bias

    def _L3_gnn_ref(x, adjacency_matrix, weight):
        import jax, jax.numpy as jnp
        import numpy as np
        N, D_IN, D_OUT = (4096, 128, 128)
        degree = jnp.sum(adjacency_matrix, axis=-1, keepdims=True)
        ax = adjacency_matrix @ x
        out = ax / degree @ weight
        return out
    h = jnp.maximum(_layernorm(x, axis=-1), 0.0)
    x = x + _L0_gnn_ref(h, adj, L0_gnn_kernel, L0_gnn_bias)
    h = jnp.maximum(_layernorm(x, axis=-1), 0.0)
    x = x + _L1_gnn_ref(h, adj, L1_gnn_W1, L1_gnn_b1, L1_gnn_W2, L1_gnn_b2)
    h = jnp.maximum(_layernorm(x, axis=-1), 0.0)
    x = x + _L2_gnn_ref(h, adj, L2_gnn_weight, L2_gnn_bias)
    h = jnp.maximum(_layernorm(x, axis=-1), 0.0)
    x = x + _L3_gnn_ref(h, adj, L3_gnn_weight)
    return x

_drawn_inputs = setup_inputs


def setup_inputs(seed=0):
    import zlib

    import numpy as np

    out = dict(_drawn_inputs(seed))
    spreads = {'L1_gnn_b1': (0.0, 0.1), 'L1_gnn_b2': (0.0, 0.505), 'L2_gnn_bias': (0.0, 0.8)}
    factors = {'L0_gnn_bias': 2.913, 'L3_gnn_weight': 8.0}
    for name, (base, spread) in spreads.items():
        noise = np.random.default_rng([zlib.crc32(name.encode()), seed]).standard_normal(out[name].shape)
        drawn = base * np.exp(spread * noise) if base else spread * noise
        out[name] = jnp.asarray(drawn.astype(out[name].dtype))
    for name, factor in factors.items():
        out[name] = (out[name] * factor).astype(out[name].dtype)
    return out
```

```python
from contextlib import ExitStack

import numpy as np

import concourse.bass as bass
from concourse import mybir

F32 = mybir.dt.float32
F32R = mybir.dt.float32r
ACT = mybir.ActivationFunctionType
ALU = mybir.AluOpType

N = 4096
P = 128
BANK = 512
SEG = 1024
SEGS = N // SEG
TILES = N // P
SUB = SEG // P
PRODUCTS = 6
EPS = 1e-5

RESIDENT = [15, 31]
RAW = 5
SPLIT = 4
STREAMED = [j for j in range(TILES) if j not in RESIDENT]
LOADS = len(STREAMED) // RAW
assert len(STREAMED) % RAW == 0 and TILES % SPLIT == 0

START = -1
NORMED = (START, 0, 2, 4)
PLAIN = (1, 3)

ACT_AT = {"evacuate": 4, "square": 9, "std": 14, "split": 18, "split_plain": 11, "spread": 16}
DVE_AT = {"residual": 5, "rstd": 15, "scale": 15, "split": 19, "split_plain": 12, "diagonal": 16,
          "normed": 21, "degree": 4, "reciprocal": 10, "divide": 17}
PE_AT = {"center": 6, "variance": 11, "weight": 11, "weight_plain": 7, "broadcast": 17,
         "degree": 6, "spread": 12}


def summed_by_pe(j, q):
    return j % 2 == 1 and j > (16 if q == 0 else 6)


def epilogues_before(kinds, kind):
    return SEGS * sum(k in kinds for k in range(START, kind))


def build(nc, adj_tiles, x_t, weights, biases, out_t):
    ctx = ExitStack()
    with ctx:
        def sbuf(name, shape, dtype=F32):
            return ctx.enter_context(nc.sbuf_tensor(name, shape, dtype))

        def psum(name, shape):
            return ctx.enter_context(nc.psum_tensor(name, shape, F32))

        def semaphore(name):
            return ctx.enter_context(nc.semaphore(name))

        g_high = [sbuf(f"g_high{i}", [P, N], F32R) for i in range(2)]
        g_low = [sbuf(f"g_low{i}", [P, N], F32R) for i in range(2)]
        x = sbuf("x", [P, N])
        h2 = sbuf("h2", [P, N])
        kept = sbuf("kept", [P, len(RESIDENT), N])
        raw = sbuf("raw", [P, RAW, SEG])
        a_high = sbuf("a_high", [P, SPLIT, SEG], F32R)
        a_low = sbuf("a_low", [P, SPLIT, SEG], F32R)
        scratch = sbuf("scratch", [P, SEG])
        squares = sbuf("squares", [P, SEG])
        h = sbuf("h", [P, SEG])
        w = sbuf("w", [P, len(weights), P])
        w_next = sbuf("w_next", [P, 2, P])
        b = sbuf("b", [P, len(biases)])
        identity = sbuf("identity", [P, P])
        identity_r = sbuf("identity_r", [P, P], F32R)
        centering = sbuf("centering", [P, P])
        ones = sbuf("ones", [P, P])
        average = sbuf("average", [P, 1])
        eps = sbuf("eps", [P, 1])
        std = sbuf("std", [P, SUB])
        rstd = sbuf("rstd", [P, SUB])

        acc = psum("acc", [P, 2, SEG])
        centered = psum("centered", [P, SEG])
        g_psum = psum("g_psum", [P, SEG])

        raw_loaded = [semaphore(f"raw_loaded{i}") for i in range(RAW)]
        kept_loaded = [semaphore(f"kept_loaded{i}") for i in range(len(RESIDENT))]
        x_loaded = semaphore("x_loaded")
        small_loaded = semaphore("small_loaded")
        zeroed = semaphore("zeroed")
        identity_made = semaphore("identity_made")
        constants_made = semaphore("constants_made")
        high_ready = semaphore("high_ready")
        low_ready = semaphore("low_ready")
        tile_added = semaphore("tile_added")
        tile_used = semaphore("tile_used")
        evacuated = semaphore("evacuated")
        x_ready = semaphore("x_ready")
        center_done = semaphore("center_done")
        square_ready = semaphore("square_ready")
        relu_ready = semaphore("relu_ready")
        variance_done = semaphore("variance_done")
        std_ready = semaphore("std_ready")
        rstd_ready = semaphore("rstd_ready")
        weight_done = semaphore("weight_done")
        scaled = semaphore("scaled")
        g_high_ready = semaphore("g_high_ready")
        g_ready = semaphore("g_ready")
        diagonal_ready = semaphore("diagonal_ready")
        broadcast_done = semaphore("broadcast_done")
        h2_ready = semaphore("h2_ready")
        partial_ready = semaphore("partial_ready")
        degree_done = semaphore("degree_done")
        reciprocal_ready = semaphore("reciprocal_ready")
        spread_ready = semaphore("spread_ready")
        divided = semaphore("divided")
        out_ready = semaphore("out_ready")
        out_stored = semaphore("out_stored")

        W0, W1, W2, K0, K1, K2, W3 = (w[:, i, :] for i in range(7))
        TWICE_K2, K0_LESS_K2 = w_next[:, 0, :], w_next[:, 1, :]
        WEIGHT = {START: W0, 0: W1, 1: W2, 2: TWICE_K2, 3: identity[:], 4: W3}

        def columns(tensor, q, first=0, size=SEG):
            return tensor[:, bass.ds(q * SEG + first, size)]

        def each_sub(ap):
            return ap.rearrange("p (s f) -> p s f", s=SUB)

        def spread(column):
            return column.unsqueeze(2).broadcast_to([P, SUB, P])

        def tile_count(p, q, j):
            return (p * SEGS + q) * TILES + j + 1

        def added_count(q, j, back=0):
            first = sum(not summed_by_pe(i, 0) for i in range(TILES))
            rest = sum(not summed_by_pe(i, 1) for i in range(TILES))
            if back:
                return first + (q - 1) * rest - sum(not summed_by_pe(i, 1) for i in range(j + 1, TILES))
            before = 0 if isinstance(q, int) else first + (q - 1) * rest
            return before + sum(not summed_by_pe(i, 0 if isinstance(q, int) else 1) for i in range(j + 1))

        def run_segments(engine, segment):
            for p in range(PRODUCTS):
                segment(p, 0, p - 1, SEGS - 1)
                with engine.Fori(1, SEGS) as q:
                    segment(p, q, p, q - 1)

        block = ctx.enter_context(nc.Block())

        @block.sync
        def _(sp):
            def load(p, q, j):
                if j in RESIDENT:
                    if p == 0:
                        r = RESIDENT.index(j)
                        sp.dma_start(kept[:, r, bass.ds(q * SEG, SEG)],
                                     adj_tiles[bass.ds(q * TILES + j, 1), :, :]
                                     .rearrange("t p c -> (t p) c")).then_inc(kept_loaded[r], 16)
                    return
                k = STREAMED.index(j)
                before, back = STREAMED[(k - RAW) % len(STREAMED)], int(k < RAW)
                loop = not isinstance(q, int)
                if p == PRODUCTS - 1 and (loop or not back) and not summed_by_pe(before, int(loop)):
                    sp.wait_ge(tile_added, added_count(q, before, back))
                elif p or loop or k >= RAW:
                    sp.wait_ge(low_ready, tile_count(p, q - back, before))
                source = q * TILES + j
                sp.dma_start(raw[:, k % RAW, :],
                             adj_tiles[bass.ds(source, 1), :, :]
                             .rearrange("t p c -> (t p) c")).then_inc(raw_loaded[k % RAW], 16)

            def segment(p, q, kind, done):
                for j in range(TILES):
                    load(p, q, j)

            run_segments(sp, segment)

        @block.gpsimd
        def _(pool):
            nc.gpsimd.memset(identity[:], 0.0).then_inc(zeroed, 1)
            pool.wait_ge(zeroed, 1)
            nc.gpsimd.affine_select(out=identity[:], in_=identity[:], compare_op=ALU.not_equal,
                                    fill=1.0, base=0, pattern=[[-1, P]],
                                    channel_multiplier=1).then_inc(identity_made, 1)
            with pool.Fori(0, SEGS) as q:
                pool.wait_ge(out_ready, q + 1)
                pool.dma_start(columns(out_t, q), columns(x, q)).then_inc(out_stored, 16)
                pool.wait_ge(out_stored, (q + 1) * 16)

        def tile_of(p, q, j):
            if j in RESIDENT:
                return kept[:, RESIDENT.index(j), bass.ds(q * SEG, SEG)]
            return raw[:, STREAMED.index(j) % RAW, :]

        @block.scalar
        def _(act):
            for i in range(len(weights)):
                act.dma_start(w[:, i, :], weights[i]).then_inc(small_loaded, 16)
            for i in range(len(biases)):
                act.dma_start(b[:, i:i + 1], biases[i]).then_inc(small_loaded, 16)
            with act.Fori(0, SEGS) as q:
                act.dma_start(columns(x, q), columns(x_t, q)).then_inc(x_loaded, 16)
                act.wait_ge(x_loaded, (q + 1) * 16)
            act.wait_ge(small_loaded, 16 * (len(weights) + len(biases)))
            act.wait_ge(constants_made, 1)

            def evacuate(kind, q):
                act.wait_ge(tile_used, tile_count(kind, q, TILES - 1))
                y = acc[:, q % 2, :]
                if kind == 3:
                    step = nc.scalar.activation(h[:], y, ACT.Copy)
                else:
                    bias = b[:, kind:kind + 1]
                    step = nc.scalar.activation(h[:] if kind == 1 else scratch[:], y, ACT.Relu, bias=bias)
                step.then_inc(evacuated, 1)

            def square(kind, q):
                e = epilogues_before(NORMED, kind) + q
                act.wait_ge(center_done, e + 1)
                nc.scalar.activation(squares[:], centered[:], ACT.Square).then_inc(square_ready, 1)
                nc.scalar.activation(h[:], centered[:], ACT.Relu).then_inc(relu_ready, 1)

            def deviation(kind, q):
                e = epilogues_before(NORMED, kind) + q
                act.wait_ge(variance_done, e + 1)
                nc.scalar.activation(std[:], centered[:, 0:SUB], ACT.Sqrt,
                                     bias=eps[:]).then_inc(std_ready, 1)

            def split_high(kind, q):
                if kind in NORMED:
                    act.wait_ge(scaled, epilogues_before(NORMED, kind) + q + 1)
                    source = scratch
                else:
                    act.wait_ge(weight_done, (kind + 1) * SEGS + q + 1)
                    source = g_psum
                nc.scalar.activation(columns(g_high[(kind + 1) % 2], q), source[:],
                                     ACT.Copy).then_inc(g_high_ready, 1)

            def copy_spread(q):
                act.wait_ge(degree_done, 2 * (q + 1))
                nc.scalar.activation(squares[:], g_psum[:], ACT.Copy).then_inc(spread_ready, 1)

            def epilogue(kind, q, j):
                if kind in (0, 1, 2, 3) and j == ACT_AT["evacuate"]:
                    evacuate(kind, q)
                if kind in NORMED:
                    if j == ACT_AT["square"]:
                        square(kind, q)
                    if j == ACT_AT["std"]:
                        deviation(kind, q)
                    if j == ACT_AT["split"]:
                        split_high(kind, q)
                if kind in PLAIN and j == ACT_AT["split_plain"]:
                    split_high(kind, q)
                if kind == PRODUCTS - 1 and j == ACT_AT["spread"]:
                    copy_spread(q)

            def segment(p, q, kind, done):
                for j in range(TILES):
                    if j not in RESIDENT:
                        k = STREAMED.index(j)
                        act.wait_ge(raw_loaded[k % RAW], 16 * ((p * SEGS + q) * LOADS + k // RAW + 1))
                    elif p == 0:
                        act.wait_ge(kept_loaded[RESIDENT.index(j)], 16 * (q + 1))
                    if p or not isinstance(q, int) or j >= SPLIT:
                        act.wait_ge(tile_used, tile_count(p, q, j) - SPLIT)
                    nc.scalar.activation(a_high[:, j % SPLIT, :], tile_of(p, q, j),
                                         ACT.Copy).then_inc(high_ready, 1)
                    epilogue(kind, done, j)

            with act.Fori(0, SEGS - 1) as q:
                square(START, q)
                deviation(START, q)
                split_high(START, q)
            run_segments(act, segment)
            for j in range(TILES):
                epilogue(PRODUCTS - 1, SEGS - 1, j)

        @block.vector
        def _(dve):
            dve.wait_ge(identity_made, 1)
            dve.wait_ge(small_loaded, 16 * (len(weights) + len(biases)))
            nc.vector.memset(ones[:], 1.0)
            nc.vector.memset(average[:], 1.0 / P)
            nc.vector.memset(eps[:], EPS)
            nc.vector.tensor_copy(identity_r[:], identity[:])
            nc.vector.tensor_scalar(centering[:], identity[:], 1.0 / P, None, ALU.subtract)
            nc.vector.tensor_scalar(TWICE_K2, K2, 2.0, None, ALU.mult)
            nc.vector.tensor_tensor(K0_LESS_K2, K0, K2, ALU.subtract).then_inc(constants_made, 1)

            def residual(kind, q):
                if kind == 4:
                    dve.wait_ge(tile_used, tile_count(kind, q, TILES - 1))
                    step = nc.vector.scalar_tensor_tensor(columns(x, q), acc[:, q % 2, :], b[:, 3:4],
                                                          columns(x, q), ALU.add, ALU.add)
                else:
                    dve.wait_ge(evacuated, kind * SEGS + q + 1)
                    step = nc.vector.tensor_tensor(columns(x, q), columns(x, q), scratch[:], ALU.add)
                step.then_inc(x_ready, 1)

            def inverse_deviation(kind, q):
                e = epilogues_before(NORMED, kind) + q
                dve.wait_ge(std_ready, e + 1)
                nc.vector.reciprocal(rstd[:], std[:]).then_inc(rstd_ready, 1)
                dve.wait_ge(rstd_ready, e + 1)

            def scale(kind, q):
                dve.wait_ge(weight_done, (kind + 1) * SEGS + q + 1)
                nc.vector.tensor_tensor(each_sub(scratch[:]), each_sub(g_psum[:]), spread(rstd[:]),
                                        ALU.mult).then_inc(scaled, 1)

            def split_low(kind, q):
                dve.wait_ge(g_high_ready, (kind + 1) * SEGS + q + 1)
                source = scratch if kind in NORMED else g_psum
                nc.vector.tensor_tensor(columns(g_low[(kind + 1) % 2], q), source[:],
                                        columns(g_high[(kind + 1) % 2], q).bitcast(F32),
                                        ALU.subtract).then_inc(g_ready, 1)

            def diagonal(q):
                nc.vector.tensor_tensor(each_sub(squares[:]),
                                        identity[:].unsqueeze(1).broadcast_to([P, SUB, P]),
                                        spread(rstd[:]), ALU.mult).then_inc(diagonal_ready, 1)

            def normed(q):
                dve.wait_ge(broadcast_done, q + 1)
                nc.vector.tensor_tensor(columns(h2, q), h[:], centered[:], ALU.mult).then_inc(h2_ready, 1)

            def degree_partials(q):
                dve.wait_ge(tile_used, tile_count(PRODUCTS - 1, q, TILES - 1))
                nc.vector.tensor_tensor(squares[:], columns(h2, q), centered[:],
                                        ALU.add).then_inc(partial_ready, 1)

            def degree_reciprocal(q):
                dve.wait_ge(degree_done, 2 * q + 1)
                nc.vector.reciprocal(rstd[:], g_psum[:, 0:SUB]).then_inc(reciprocal_ready, 1)
                dve.wait_ge(reciprocal_ready, 2 * q + 1)
                nc.vector.tensor_tensor(each_sub(scratch[:]),
                                        identity[:].unsqueeze(1).broadcast_to([P, SUB, P]),
                                        spread(rstd[:]), ALU.mult).then_inc(reciprocal_ready, 1)

            def divide(q):
                dve.wait_ge(spread_ready, q + 1)
                nc.vector.tensor_tensor(scratch[:], acc[:, q % 2, :], squares[:],
                                        ALU.mult).then_inc(divided, 1)
                dve.wait_ge(divided, q + 1)
                nc.vector.tensor_tensor(columns(x, q), columns(x, q), scratch[:],
                                        ALU.add).then_inc(out_ready, 1)

            def epilogue(kind, q, j):
                if kind in (0, 2, 4) and j == DVE_AT["residual"]:
                    residual(kind, q)
                if kind in NORMED:
                    if j == DVE_AT["rstd"]:
                        inverse_deviation(kind, q)
                        scale(kind, q)
                    if kind == 2 and j == DVE_AT["diagonal"]:
                        diagonal(q)
                    if j == DVE_AT["split"]:
                        split_low(kind, q)
                    if kind == 2 and j == DVE_AT["normed"]:
                        normed(q)
                if kind in PLAIN and j == DVE_AT["split_plain"]:
                    split_low(kind, q)
                if kind == PRODUCTS - 1:
                    if j == DVE_AT["degree"]:
                        degree_partials(q)
                    if j == DVE_AT["reciprocal"]:
                        degree_reciprocal(q)
                    if j == DVE_AT["divide"]:
                        divide(q)

            def segment(p, q, kind, done):
                for j in range(TILES):
                    tile = tile_of(p, q, j)
                    dve.wait_ge(high_ready, tile_count(p, q, j))
                    nc.vector.tensor_tensor(a_low[:, j % SPLIT, :], tile,
                                            a_high[:, j % SPLIT, :].bitcast(F32),
                                            ALU.subtract).then_inc(low_ready, 1)
                    if p == PRODUCTS - 1 and not summed_by_pe(j, q if isinstance(q, int) else 1):
                        if j == 0:
                            step = nc.vector.tensor_copy(columns(h2, q), tile)
                        else:
                            dve.wait_ge(tile_added, added_count(q, j) - 1)
                            step = nc.vector.tensor_tensor(columns(h2, q), columns(h2, q), tile, ALU.add)
                        step.then_inc(tile_added, 1)
                    epilogue(kind, done, j)

            with dve.Fori(0, SEGS - 1) as q:
                inverse_deviation(START, q)
                scale(START, q)
                split_low(START, q)
            run_segments(dve, segment)
            for j in range(TILES):
                epilogue(PRODUCTS - 1, SEGS - 1, j)

        @block.tensor
        def _(pe):
            pe.wait_ge(constants_made, 1)

            def halves(out, lhsT, rhs, start=True, stop=True):
                for s in range(0, SEG, BANK):
                    last = nc.tensor.matmul(out[:, s:s + BANK], lhsT, rhs(s), start=start, stop=stop)
                return last

            def center(kind, q):
                e = epilogues_before(NORMED, kind) + q
                if kind > START or not isinstance(q, int) or q:
                    pe.wait_ge(std_ready, e)
                if kind == START:
                    pe.wait_ge(x_loaded, (q + 1) * 16)
                else:
                    pe.wait_ge(x_ready, epilogues_before((0, 2, 4), kind) + q + 1)
                halves(centered, centering[:], lambda s: columns(x, q, s, BANK)).then_inc(center_done, 1)

            def variance(kind, q):
                e = epilogues_before(NORMED, kind) + q
                pe.wait_ge(square_ready, e + 1)
                pe.wait_ge(relu_ready, e + 1)
                for s in range(SUB):
                    last = nc.tensor.matmul(centered[:, s:s + 1], squares[:, s * P:s * P + P], average[:],
                                            start=True, stop=True)
                last.then_inc(variance_done, 1)

            def weight(kind, q):
                if kind in PLAIN:
                    pe.wait_ge(evacuated, kind * SEGS + q + 1)
                for s in range(SUB):
                    last = nc.tensor.matmul(g_psum[:, s * P:s * P + P], h[:, s * P:s * P + P],
                                            WEIGHT[kind], start=True, stop=True)
                last.then_inc(weight_done, 1)

            def broadcast(q):
                pe.wait_ge(diagonal_ready, q + 1)
                halves(centered, ones[:], lambda s: squares[:, s:s + BANK]).then_inc(broadcast_done, 1)

            def degree(q):
                pe.wait_ge(partial_ready, q + 1)
                for s in range(SUB):
                    last = nc.tensor.matmul(g_psum[:, s:s + 1], squares[:, s * P:s * P + P], ones[:, 0:1],
                                            start=True, stop=True)
                last.then_inc(degree_done, 1)

            def spread_degree(q):
                pe.wait_ge(reciprocal_ready, 2 * (q + 1))
                halves(g_psum, ones[:], lambda s: scratch[:, s:s + BANK]).then_inc(degree_done, 1)

            def epilogue(kind, q, j):
                if kind in NORMED:
                    if j == PE_AT["center"]:
                        center(kind, q)
                    if j == PE_AT["variance"]:
                        variance(kind, q)
                        weight(kind, q)
                    if kind == 2 and j == PE_AT["broadcast"]:
                        broadcast(q)
                if kind in PLAIN and j == PE_AT["weight_plain"]:
                    weight(kind, q)
                if kind == PRODUCTS - 1:
                    if j == PE_AT["degree"]:
                        degree(q)
                    if j == PE_AT["spread"]:
                        spread_degree(q)

            def segment(p, q, kind, done):
                y = acc[:, q % 2, :]
                summed = [j for j in range(TILES) if summed_by_pe(j, q if isinstance(q, int) else 1)]
                if not isinstance(q, int):
                    pe.wait_ge(g_ready, (p + 1) * SEGS)
                for j in range(TILES):
                    if isinstance(q, int) and j % SUB == 0:
                        pe.wait_ge(g_ready, p * SEGS + j // SUB + 1)
                    high = g_high[p % 2][:, j * P:j * P + P]
                    low = g_low[p % 2][:, j * P:j * P + P]
                    first, last = j == 0, j == TILES - 1
                    if last and p in (3, 4):
                        pe.wait_ge(h2_ready, q + 1)
                        halves(y, K1 if p == 3 else K0_LESS_K2, lambda s: columns(h2, q, s, BANK),
                               start=False, stop=False)
                    pe.wait_ge(low_ready, tile_count(p, q, j))
                    for part, a, g in ((0, a_high, high), (1, a_low, high), (2, a_high, low)):
                        for s in range(0, SEG, BANK):
                            step = nc.tensor.matmul(
                                y[:, s:s + BANK], g, a[:, j % SPLIT, s:s + BANK],
                                start=first and part == 0, stop=last and part == 2)
                    if p == PRODUCTS - 1 and j in summed:
                        for a in (a_high, a_low):
                            for s in range(0, SEG, BANK):
                                step = nc.tensor.matmul(
                                    centered[:, s:s + BANK], identity_r[:], a[:, j % SPLIT, s:s + BANK],
                                    start=j == summed[0] and a is a_high,
                                    stop=j == summed[-1] and a is a_low)
                    step.then_inc(tile_used, 1)
                    epilogue(kind, done, j)

            center(START, 0)
            variance(START, 0)
            weight(START, 0)
            with pe.Fori(1, SEGS - 1) as q:
                center(START, q)
                variance(START, q)
                weight(START, q)
            run_segments(pe, segment)
            for j in range(TILES):
                epilogue(PRODUCTS - 1, SEGS - 1, j)


def kernel(x, adj, L0_gnn_kernel, L0_gnn_bias, L1_gnn_W1, L1_gnn_b1, L1_gnn_W2, L1_gnn_b2,
           L2_gnn_weight, L2_gnn_bias, L3_gnn_weight):
    import concourse.bacc as bacc
    from concourse.bass_utils import run_bass_kernel_spmd

    nc = bacc.Bacc("TRN2", target_bir_lowering=False, num_devices=1)
    arrays = {}

    def give(name, array):
        arrays[name] = np.ascontiguousarray(array)
        return nc.dram_tensor(name, arrays[name].shape, F32, kind="ExternalInput").ap()

    tiles = np.asarray(adj).reshape(SEGS, SEG, TILES, P).transpose(0, 2, 3, 1)
    adj_tiles = give("adj_tiles", tiles.reshape(SEGS * TILES, P, SEG))
    x_t = give("x_t", np.asarray(x).T)
    chebyshev = np.asarray(L2_gnn_weight)
    matrices = [L0_gnn_kernel, L1_gnn_W1, L1_gnn_W2, chebyshev[0], chebyshev[1], chebyshev[2], L3_gnn_weight]
    weights = [give(f"weight{i}", m) for i, m in enumerate(matrices)]
    columns = [L0_gnn_bias, L1_gnn_b1, L1_gnn_b2, L2_gnn_bias]
    biases = [give(f"bias{i}", np.asarray(c)[:, None]) for i, c in enumerate(columns)]
    out_t = nc.dram_tensor("out_t", (P, N), F32, kind="ExternalOutput").ap()
    build(nc, adj_tiles, x_t, weights, biases, out_t)
    result = run_bass_kernel_spmd(nc, [arrays], core_ids=[0])
    return np.ascontiguousarray(result.results[0]["out_t"].T)
```

```python
from contextlib import ExitStack

import numpy as np

import concourse.bass as bass
from concourse import mybir

F32 = mybir.dt.float32
F32R = mybir.dt.float32r
ACT = mybir.ActivationFunctionType
ALU = mybir.AluOpType

N = 4096
P = 128
BANK = 512
SEG = 1024
SEGS = N // SEG
TILES = N // P
SUB = SEG // P
PRODUCTS = 6
EPS = 1e-5
WEIGHTS = 7
BIASES = 4

RESIDENT = [15, 31]
RAW = 5
SPLIT = 5
STREAMED = [j for j in range(TILES) if j not in RESIDENT]
LOADS = len(STREAMED) // RAW
assert len(STREAMED) % RAW == 0 and len(STREAMED) % SPLIT == 0

SUMMED = {0: (1, 19, 25, 28, 31), 1: (4, 21, 22, 26, 29), 2: (3, 15, 24), 4: (6, 18, 20, 27, 30),
          5: (0, 2, 5, 7, 8, 9, 10, 11, 12, 13, 14, 16, 17, 23)}
SUMMED_BY_PE = (8, 10, 12, 14, 16)
assert sorted(sum(SUMMED.values(), ())) == list(range(TILES))

START = -1
NORMED = (START, 0, 2, 4)
PLAIN = (1, 3)

NORM = [("center", 7), ("square", 10), ("variance", 12), ("weight", 12), ("deviation", 17),
        ("inverse_deviation", 17), ("scale", 19), ("scale_rest", 20), ("split_high", 21),
        ("split_low", 22)]
WEIGHT_ONLY = [("evacuate", 4), ("weight", 7), ("split_high", 11), ("split_low", 12)]
STEPS = {
    0: [("evacuate", 4), ("residual", 5)] + NORM,
    1: WEIGHT_ONLY,
    2: [("evacuate", 4), ("residual", 5)] + NORM
       + [("diagonal", 18), ("broadcast", 23), ("normed", 28)],
    3: WEIGHT_ONLY,
    4: [("residual", 5)] + NORM,
    5: [("divide", 3)],
}
START_STEPS = {
    2: [("center", 0), ("square", 4), ("variance", 6), ("weight", 6), ("deviation", 10),
        ("inverse_deviation", 10), ("scale", 11), ("scale_rest", 12), ("split_high", 12),
        ("split_low", 13)],
    3: [("center", 8), ("square", 13), ("variance", 15), ("weight", 15), ("deviation", 19),
        ("inverse_deviation", 19), ("scale", 20), ("scale_rest", 20), ("split_high", 21),
        ("split_low", 22)],
}
OWN_STEPS = {
    2: [("degree", 26), ("keep_degree", 31)],
    5: [("merge", 20), ("degree", 24), ("inverse_degree", 28), ("spread_degree", 29),
        ("copy_degree", 31)],
}


def steps_after(p, q, j):
    first = isinstance(q, int)
    if p == 0 and first:
        steps = [(s, START, quarter) for quarter in START_STEPS
                 for s, at in START_STEPS[quarter] if at == j]
    else:
        kind, done = (p - 1, SEGS - 1) if first else (p, q - 1)
        steps = [(s, kind, done) for s, at in STEPS[kind] if at == j]
    return steps + [(s, p, q) for s, at in OWN_STEPS.get(p, []) if at == j]


def added_by_dve(p):
    return [j for j in SUMMED.get(p, ()) if p < PRODUCTS - 1 or j not in SUMMED_BY_PE]


def epilogues_before(kinds, kind):
    return SEGS * sum(k in kinds for k in range(START, kind))


def build(nc, adj_tiles, x_t, weights, biases, out_t):
    ctx = ExitStack()
    with ctx:
        def sbuf(name, shape, dtype=F32):
            return ctx.enter_context(nc.sbuf_tensor(name, shape, dtype))

        def psum(name, shape):
            return ctx.enter_context(nc.psum_tensor(name, shape, F32))

        def semaphore(name):
            return ctx.enter_context(nc.semaphore(name))

        g_high = [sbuf(f"g_high{i}", [P, N], F32R) for i in range(2)]
        g_low = [sbuf(f"g_low{i}", [P, N], F32R) for i in range(2)]
        g_full = [sbuf(f"g_full{i}", [P, len(RESIDENT) * P]) for i in range(2)]
        x = sbuf("x", [P, N])
        h2 = sbuf("h2", [P, N])
        kept = sbuf("kept", [P, len(RESIDENT), N])
        raw = sbuf("raw", [P, RAW, SEG])
        a_high = sbuf("a_high", [P, SPLIT, SEG], F32R)
        a_low = sbuf("a_low", [P, SPLIT, SEG], F32R)
        scratch = sbuf("scratch", [P, SEG])
        squares = sbuf("squares", [P, SEG])
        h = sbuf("h", [P, SEG])
        w = sbuf("w", [P, WEIGHTS, P])
        b = sbuf("b", [P, BIASES])
        identity = sbuf("identity", [P, P])
        identity_r = sbuf("identity_r", [P, P], F32R)
        centering = sbuf("centering", [P, P])
        ones = sbuf("ones", [P, P])
        average = sbuf("average", [P, 1])
        eps = sbuf("eps", [P, 1])
        std = sbuf("std", [P, SUB])
        rstd = sbuf("rstd", [P, SUB])
        degrees = sbuf("degrees", [P, SEGS * SUB])
        inverse = sbuf("inverse", [P, SUB])

        acc = psum("acc", [P, 2, SEG])
        centered = psum("centered", [P, SEG])
        g_psum = psum("g_psum", [P, SEG])

        raw_loaded = [semaphore(f"raw_loaded{i}") for i in range(RAW)]
        kept_loaded = [semaphore(f"kept_loaded{i}") for i in range(len(RESIDENT))]
        x_loaded = [semaphore(f"x_loaded{i}") for i in range(SEGS)]
        small_loaded = semaphore("small_loaded")
        zeroed = semaphore("zeroed")
        identity_made = semaphore("identity_made")
        constants_made = semaphore("constants_made")
        high_ready = semaphore("high_ready")
        low_ready = semaphore("low_ready")
        tile_added = semaphore("tile_added")
        tile_used = semaphore("tile_used")
        evacuated = semaphore("evacuated")
        x_ready = semaphore("x_ready")
        center_done = semaphore("center_done")
        square_ready = semaphore("square_ready")
        relu_ready = semaphore("relu_ready")
        variance_done = semaphore("variance_done")
        std_ready = semaphore("std_ready")
        rstd_ready = semaphore("rstd_ready")
        weight_done = semaphore("weight_done")
        scaled = semaphore("scaled")
        g_high_ready = semaphore("g_high_ready")
        g_full_ready = semaphore("g_full_ready")
        g_ready = semaphore("g_ready")
        diagonal_ready = semaphore("diagonal_ready")
        broadcast_done = semaphore("broadcast_done")
        h2_ready = semaphore("h2_ready")
        h2_used = semaphore("h2_used")
        merged = semaphore("merged")
        degree_done = semaphore("degree_done")
        degree_kept = semaphore("degree_kept")
        degree_summed = semaphore("degree_summed")
        inverse_ready = semaphore("inverse_ready")
        inverse_diagonal = semaphore("inverse_diagonal")
        spread_done = semaphore("spread_done")
        spread_ready = semaphore("spread_ready")
        divided = semaphore("divided")
        out_ready = semaphore("out_ready")
        out_stored = semaphore("out_stored")

        W0, W1, W2, K0, K1, K2, W3 = (w[:, i, :] for i in range(7))
        TWICE_K2, K0_LESS_K2 = K2, K0
        WEIGHT = {START: W0, 0: W1, 1: W2, 2: TWICE_K2, 3: identity[:], 4: W3}

        def columns(tensor, q, first=0, size=SEG):
            return tensor[:, bass.ds(q * SEG + first, size)]

        def each_sub(ap):
            return ap.rearrange("p (s f) -> p s f", s=SUB)

        def spread(column):
            return column.unsqueeze(2).broadcast_to([P, SUB, P])

        def tile_count(p, q, j):
            return (p * SEGS + q) * TILES + j + 1

        def split_count(p, q, j):
            return (p * SEGS + q) * len(STREAMED) + STREAMED.index(j % TILES) + 1 - (
                len(STREAMED) if j < 0 else 0)

        def added_count(p, q, j):
            if j < 0:
                owner = p - 1 if isinstance(q, int) else p
                return added_count(p, q, 0) - (0 in added_by_dve(p)) - sum(
                    i > j + TILES for i in added_by_dve(owner))
            before = SEGS * sum(len(added_by_dve(i)) for i in range(p))
            return before + q * len(added_by_dve(p)) + sum(i <= j for i in added_by_dve(p))

        def pe_sums(q):
            return acc[:, 1, :] if isinstance(q, int) else centered[:]

        def start_buffers(kind, q):
            if kind == START and q % 2:
                return acc[:, 1, :], h2[:, 2 * SEG:3 * SEG], h2[:, 3 * SEG:4 * SEG]
            return centered[:], squares[:], h[:]

        def run_segments(engine, segment):
            for p in range(PRODUCTS):
                segment(p, 0)
                with engine.Fori(1, SEGS) as q:
                    segment(p, q)

        block = ctx.enter_context(nc.Block())

        @block.sync
        def _(sp):
            def segment(p, q):
                first = isinstance(q, int)
                for j in range(TILES):
                    source = adj_tiles[bass.ds(q * TILES + j, 1), :, :].rearrange("t p c -> (t p) c")
                    if j in RESIDENT:
                        if p == 0:
                            r = RESIDENT.index(j)
                            sp.dma_start(kept[:, r, bass.ds(q * SEG, SEG)], source).then_inc(kept_loaded[r], 16)
                        continue
                    k = STREAMED.index(j)
                    if p or not first or k >= RAW:
                        before = STREAMED[k - RAW] - (TILES if k < RAW else 0)
                        owner = p - 1 if k < RAW and first else p
                        if before % TILES in added_by_dve(owner):
                            sp.wait_ge(tile_added, added_count(p, q, before))
                        else:
                            sp.wait_ge(low_ready, split_count(p, q, before))
                    sp.dma_start(raw[:, k % RAW, :], source).then_inc(raw_loaded[k % RAW], 16)

            sp.dma_start(columns(x, 0), columns(x_t, 0)).then_inc(x_loaded[0], 16)
            run_segments(sp, segment)

        @block.gpsimd
        def _(pool):
            nc.gpsimd.memset(identity[:], 0.0).then_inc(zeroed, 1)
            pool.wait_ge(zeroed, 1)
            nc.gpsimd.affine_select(out=identity[:], in_=identity[:], compare_op=ALU.not_equal,
                                    fill=1.0, base=0, pattern=[[-1, P]],
                                    channel_multiplier=1).then_inc(identity_made, 1)
            with pool.Fori(0, SEGS) as q:
                pool.wait_ge(out_ready, q + 1)
                pool.dma_start(columns(out_t, q), columns(x, q)).then_inc(out_stored, 16)
                pool.wait_ge(out_stored, (q + 1) * 16)

        @block.scalar
        def _(act):
            act.dma_start(w[:], weights).then_inc(small_loaded, 16)
            act.dma_start(b[:], biases).then_inc(small_loaded, 16)
            for q in range(1, SEGS):
                act.dma_start(columns(x, q), columns(x_t, q)).then_inc(x_loaded[q], 16)
            act.wait_ge(constants_made, 2)

            def evacuate(kind, q):
                act.wait_ge(tile_used, tile_count(kind, q, TILES - 1))
                y = acc[:, q % 2, :]
                if kind == 3:
                    step = nc.scalar.activation(h[:], y, ACT.Copy)
                else:
                    bias = b[:, kind:kind + 1]
                    step = nc.scalar.activation(h[:] if kind == 1 else scratch[:], y, ACT.Relu, bias=bias)
                step.then_inc(evacuated, 1)

            def square(kind, q):
                e = epilogues_before(NORMED, kind) + q
                act.wait_ge(center_done, e + 1)
                source, squared, positive = start_buffers(kind, q)
                nc.scalar.activation(squared, source, ACT.Square).then_inc(square_ready, 1)
                nc.scalar.activation(positive, source, ACT.Relu).then_inc(relu_ready, 1)

            def deviation(kind, q):
                e = epilogues_before(NORMED, kind) + q
                act.wait_ge(variance_done, e + 1)
                nc.scalar.activation(std[:], start_buffers(kind, q)[0][:, 0:SUB], ACT.Sqrt,
                                     bias=eps[:]).then_inc(std_ready, 1)

            def scale(kind, q, subs=range(SUB // 2)):
                act.wait_ge(weight_done, (kind + 1) * SEGS + q + 1)
                act.wait_ge(rstd_ready, epilogues_before(NORMED, kind) + q + 1)
                if kind == START and q:
                    act.wait_ge(g_ready, q)
                for s in subs:
                    nc.scalar.activation(each_sub(scratch[:])[:, s, :], each_sub(g_psum[:])[:, s, :],
                                         ACT.Copy, scale=rstd[:, s:s + 1]).then_inc(scaled, 1)

            def scale_rest(kind, q):
                scale(kind, q, range(SUB // 2, SUB))

            def split_high(kind, q):
                if kind in NORMED:
                    act.wait_ge(scaled, SUB * (epilogues_before(NORMED, kind) + q + 1))
                    source = scratch
                else:
                    act.wait_ge(weight_done, (kind + 1) * SEGS + q + 1)
                    source = g_psum
                nc.scalar.activation(g_full[(kind + 1) % 2][:, bass.ds(q // 2 * P, P)],
                                     source[:, SEG - P:SEG], ACT.Copy).then_inc(g_full_ready, 1)
                nc.scalar.activation(columns(g_high[(kind + 1) % 2], q), source[:],
                                     ACT.Copy).then_inc(g_high_ready, 1)

            def copy_degree(kind, q):
                act.wait_ge(spread_done, q + 1)
                nc.scalar.activation(squares[:], centered[:], ACT.Copy).then_inc(spread_ready, 1)

            steps = dict(evacuate=evacuate, square=square, deviation=deviation, scale=scale,
                         scale_rest=scale_rest,                         split_high=split_high, copy_degree=copy_degree)

            def segment(p, q):
                for j in range(TILES):
                    if j not in RESIDENT:
                        k = STREAMED.index(j)
                        act.wait_ge(raw_loaded[k % RAW], 16 * ((p * SEGS + q) * LOADS + k // RAW + 1))
                        if p or not isinstance(q, int) or k >= SPLIT:
                            before = STREAMED[k - SPLIT] - (TILES if k < SPLIT else 0)
                            act.wait_ge(tile_used, tile_count(p, q, before))
                        nc.scalar.activation(a_high[:, k % SPLIT, :], raw[:, k % RAW, :],
                                             ACT.Copy).then_inc(high_ready, 1)
                    for step, kind, done in steps_after(p, q, j):
                        if step in steps:
                            steps[step](kind, done)

            square(START, 0)
            square(START, 1)
            for q in range(2):
                deviation(START, q)
                scale(START, q)
                scale_rest(START, q)
                split_high(START, q)
            run_segments(act, segment)

        @block.vector
        def _(dve):
            dve.wait_ge(identity_made, 1)
            dve.wait_ge(small_loaded, 32)
            nc.vector.memset(ones[:], 1.0)
            nc.vector.memset(average[:], 1.0 / P)
            nc.vector.memset(eps[:], EPS)
            nc.vector.tensor_copy(identity_r[:], identity[:])
            nc.vector.tensor_scalar(centering[:], identity[:], 1.0 / P, None, ALU.subtract)
            nc.vector.tensor_tensor(K0_LESS_K2, K0, K2, ALU.subtract).then_inc(constants_made, 1)
            dve.wait_ge(constants_made, 1)
            nc.vector.tensor_scalar(TWICE_K2, K2, 2.0, None, ALU.mult).then_inc(constants_made, 1)

            def residual(kind, q):
                if kind == 4:
                    dve.wait_ge(tile_used, tile_count(kind, q, TILES - 1))
                    step = nc.vector.scalar_tensor_tensor(columns(x, q), acc[:, q % 2, :], b[:, 3:4],
                                                          columns(x, q), ALU.add, ALU.add)
                else:
                    dve.wait_ge(evacuated, kind * SEGS + q + 1)
                    step = nc.vector.tensor_tensor(columns(x, q), columns(x, q), scratch[:], ALU.add)
                step.then_inc(x_ready, 1)

            def inverse_deviation(kind, q):
                e = epilogues_before(NORMED, kind) + q
                dve.wait_ge(std_ready, e + 1)
                if kind == START and q:
                    dve.wait_ge(scaled, SUB * q)
                nc.vector.reciprocal(rstd[:], std[:]).then_inc(rstd_ready, 1)
                dve.wait_ge(rstd_ready, e + 1)

            def split_low(kind, q):
                dve.wait_ge(g_high_ready, (kind + 1) * SEGS + q + 1)
                source = scratch if kind in NORMED else g_psum
                nc.vector.tensor_tensor(columns(g_low[(kind + 1) % 2], q), source[:],
                                        columns(g_high[(kind + 1) % 2], q).bitcast(F32),
                                        ALU.subtract).then_inc(g_ready, 1)

            def diagonal(kind, q):
                nc.vector.tensor_tensor(each_sub(squares[:]),
                                        identity[:].unsqueeze(1).broadcast_to([P, SUB, P]),
                                        spread(rstd[:]), ALU.mult).then_inc(diagonal_ready, 1)

            def normed(kind, q):
                dve.wait_ge(broadcast_done, q + 1)
                nc.vector.tensor_tensor(columns(h2, q), h[:], centered[:], ALU.mult).then_inc(h2_ready, 1)

            def merge(p, q):
                dve.wait_ge(tile_used, tile_count(p, q, SUMMED_BY_PE[-1]))
                dve.wait_ge(tile_added, added_count(p, q, dict(OWN_STEPS[5])["merge"]))
                nc.vector.tensor_tensor(columns(h2, q), columns(h2, q), pe_sums(q),
                                        ALU.add).then_inc(merged, 1)

            def keep_degree(p, q):
                dve.wait_ge(degree_done, q + 1)
                nc.vector.tensor_copy(degrees[:, bass.ds(q * SUB, SUB)],
                                      g_psum[:, 0:SUB]).then_inc(degree_kept, 1)

            def inverse_degree(p, q):
                dve.wait_ge(degree_done, SEGS + q + 1)
                nc.vector.tensor_tensor(inverse[:], degrees[:, bass.ds(q * SUB, SUB)],
                                        centered[:, 0:SUB], ALU.add).then_inc(degree_summed, 1)
                dve.wait_ge(degree_summed, q + 1)
                nc.vector.reciprocal(inverse[:], inverse[:]).then_inc(inverse_ready, 1)
                dve.wait_ge(inverse_ready, q + 1)
                nc.vector.tensor_tensor(each_sub(scratch[:]),
                                        identity[:].unsqueeze(1).broadcast_to([P, SUB, P]),
                                        spread(inverse[:]), ALU.mult).then_inc(inverse_diagonal, 1)

            def divide(p, q):
                dve.wait_ge(tile_used, tile_count(p, q, TILES - 1))
                dve.wait_ge(spread_ready, q + 1)
                nc.vector.tensor_tensor(scratch[:], acc[:, q % 2, :], squares[:],
                                        ALU.mult).then_inc(divided, 1)
                dve.wait_ge(divided, q + 1)
                nc.vector.tensor_tensor(columns(x, q), columns(x, q), scratch[:],
                                        ALU.add).then_inc(out_ready, 1)

            def add_tile(p, q, j):
                mine = added_by_dve(p)
                if p == 0 and j in RESIDENT:
                    dve.wait_ge(kept_loaded[RESIDENT.index(j)], 16 * (q + 1))
                tile = kept[:, RESIDENT.index(j), bass.ds(q * SEG, SEG)] if j in RESIDENT else (
                    raw[:, STREAMED.index(j) % RAW, :])
                if p in (0, 4) and j == mine[0]:
                    if p == 4:
                        dve.wait_ge(h2_used, q + 1)
                    step = nc.vector.tensor_copy(columns(h2, q), tile)
                else:
                    dve.wait_ge(tile_added, added_count(p, q, j) - 1)
                    if p == 5 and j == mine[-1]:
                        dve.wait_ge(merged, q + 1)
                    if p in (2, 5) and j == mine[-1] and (p == 2 or isinstance(q, int)):
                        dve.wait_ge(g_ready, (p + 1) * SEGS + q)
                    out = scratch[:] if p in (2, 5) and j == mine[-1] else columns(h2, q)
                    step = nc.vector.tensor_tensor(out, columns(h2, q), tile, ALU.add)
                step.then_inc(tile_added, 1)

            steps = dict(residual=residual, inverse_deviation=inverse_deviation, split_low=split_low, diagonal=diagonal, normed=normed, merge=merge,
                         keep_degree=keep_degree, inverse_degree=inverse_degree, divide=divide)

            def segment(p, q):
                for j in range(TILES):
                    if j not in RESIDENT:
                        k = STREAMED.index(j)
                        dve.wait_ge(high_ready, split_count(p, q, j))
                        nc.vector.tensor_tensor(a_low[:, k % SPLIT, :], raw[:, k % RAW, :],
                                                a_high[:, k % SPLIT, :].bitcast(F32),
                                                ALU.subtract).then_inc(low_ready, 1)
                    if j in added_by_dve(p):
                        add_tile(p, q, j)
                    for step, kind, done in steps_after(p, q, j):
                        if step in steps:
                            steps[step](kind, done)

            for q in range(2):
                inverse_deviation(START, q)
                split_low(START, q)
            run_segments(dve, segment)
            divide(PRODUCTS - 1, SEGS - 1)

        @block.tensor
        def _(pe):
            pe.wait_ge(constants_made, 2)

            def halves(out, lhsT, rhs, start=True, stop=True):
                for s in range(0, SEG, BANK):
                    last = nc.tensor.matmul(out[:, s:s + BANK], lhsT, rhs(s), start=start, stop=stop)
                return last

            def center(kind, q):
                e = epilogues_before(NORMED, kind) + q
                if kind > START or q > 1:
                    pe.wait_ge(std_ready, e if kind > START else q - 1)
                if kind == START:
                    pe.wait_ge(x_loaded[q], 16)
                else:
                    pe.wait_ge(x_ready, epilogues_before((0, 2, 4), kind) + q + 1)
                halves(start_buffers(kind, q)[0], centering[:], lambda s: columns(x, q, s, BANK)).then_inc(center_done, 1)

            def variance(kind, q):
                e = epilogues_before(NORMED, kind) + q
                pe.wait_ge(square_ready, e + 1)
                pe.wait_ge(relu_ready, e + 1)
                out, squared, _ = start_buffers(kind, q)
                for s in range(SUB):
                    last = nc.tensor.matmul(out[:, s:s + 1], squared[:, s * P:s * P + P], average[:],
                                            start=True, stop=True)
                last.then_inc(variance_done, 1)

            def weight(kind, q):
                if kind in PLAIN:
                    pe.wait_ge(evacuated, kind * SEGS + q + 1)
                if kind == START and q:
                    pe.wait_ge(scaled, SUB * q)
                source = start_buffers(kind, q)[2]
                for s in range(SUB):
                    last = nc.tensor.matmul(g_psum[:, s * P:s * P + P], source[:, s * P:s * P + P],
                                            WEIGHT[kind], start=True, stop=True)
                last.then_inc(weight_done, 1)

            def broadcast(kind, q):
                pe.wait_ge(diagonal_ready, q + 1)
                halves(centered, ones[:], lambda s: squares[:, s:s + BANK]).then_inc(broadcast_done, 1)

            def degree(p, q):
                pe.wait_ge(tile_added, added_count(p, q, added_by_dve(p)[-1]))
                if p == 5 and isinstance(q, int):
                    pe.wait_ge(std_ready, SEGS * len(NORMED))
                out = g_psum if p == 2 else centered
                for s in range(SUB):
                    last = nc.tensor.matmul(out[:, s:s + 1], scratch[:, s * P:s * P + P], ones[:, 0:1],
                                            start=True, stop=True)
                last.then_inc(degree_done, 1)

            def spread_degree(p, q):
                pe.wait_ge(inverse_diagonal, q + 1)
                halves(centered, ones[:], lambda s: scratch[:, s:s + BANK]).then_inc(spread_done, 1)

            steps = dict(center=center, variance=variance, weight=weight, broadcast=broadcast,
                         degree=degree, spread_degree=spread_degree)

            def segment(p, q):
                first = isinstance(q, int)
                y = acc[:, q % 2, :]
                for j in range(TILES):
                    if first and j % SUB == 0:
                        pe.wait_ge(g_ready, p * SEGS + j // SUB + 1)
                    if j in RESIDENT:
                        r = RESIDENT.index(j)
                        if p == 0:
                            pe.wait_ge(kept_loaded[r], 16 * (q + 1))
                        step = halves(y, g_full[p % 2][:, r * P:r * P + P],
                                      lambda s: kept[:, r, bass.ds(q * SEG + s, BANK)],
                                      start=False, stop=j == TILES - 1)
                    else:
                        k = STREAMED.index(j)
                        high = g_high[p % 2][:, j * P:j * P + P]
                        low = g_low[p % 2][:, j * P:j * P + P]
                        pe.wait_ge(low_ready, split_count(p, q, j))
                        for part, a, g in ((0, a_high, high), (1, a_low, high), (2, a_high, low)):
                            for s in range(0, SEG, BANK):
                                step = nc.tensor.matmul(y[:, s:s + BANK], g, a[:, k % SPLIT, s:s + BANK],
                                                        start=j == 0 and part == 0, stop=False)
                    if p == PRODUCTS - 1 and j in SUMMED_BY_PE:
                        if j == SUMMED_BY_PE[0]:
                            if first:
                                pe.wait_ge(x_ready, 3 * SEGS)
                            else:
                                pe.wait_ge(spread_ready, q)
                        for a in (a_high, a_low):
                            for s in range(0, SEG, BANK):
                                step = nc.tensor.matmul(
                                    pe_sums(q)[:, s:s + BANK], identity_r[:], a[:, k % SPLIT, s:s + BANK],
                                    start=j == SUMMED_BY_PE[0] and a is a_high,
                                    stop=j == SUMMED_BY_PE[-1] and a is a_low)
                    step.then_inc(tile_used, 1)
                    if p in (3, 4) and j == 1:
                        pe.wait_ge(h2_ready, q + 1)
                        step = halves(y, K1 if p == 3 else K0_LESS_K2,
                                      lambda s: columns(h2, q, s, BANK), start=False, stop=False)
                        if p == 4:
                            step.then_inc(h2_used, 1)
                    for step, kind, done in steps_after(p, q, j):
                        if step in steps:
                            steps[step](kind, done)

            center(START, 0)
            center(START, 1)
            for q in range(2):
                variance(START, q)
                weight(START, q)
            run_segments(pe, segment)


def kernel(x, adj, L0_gnn_kernel, L0_gnn_bias, L1_gnn_W1, L1_gnn_b1, L1_gnn_W2, L1_gnn_b2,
           L2_gnn_weight, L2_gnn_bias, L3_gnn_weight):
    import concourse.bacc as bacc
    from concourse.bass_utils import run_bass_kernel_spmd

    nc = bacc.Bacc("TRN2", target_bir_lowering=False, num_devices=1)
    arrays = {}

    def give(name, array):
        arrays[name] = np.ascontiguousarray(array)
        return nc.dram_tensor(name, arrays[name].shape, F32, kind="ExternalInput").ap()

    tiles = np.asarray(adj).reshape(SEGS, SEG, TILES, P).transpose(0, 2, 3, 1)
    adj_tiles = give("adj_tiles", tiles.reshape(SEGS * TILES, P, SEG))
    x_t = give("x_t", np.asarray(x).T)
    chebyshev = np.asarray(L2_gnn_weight)
    matrices = [L0_gnn_kernel, L1_gnn_W1, L1_gnn_W2, chebyshev[0], chebyshev[1], chebyshev[2], L3_gnn_weight]
    weights = give("weights", np.stack([np.asarray(m) for m in matrices], axis=1))
    vectors = [L0_gnn_bias, L1_gnn_b1, L1_gnn_b2, L2_gnn_bias]
    biases = give("biases", np.stack([np.asarray(v) for v in vectors], axis=1))
    out_t = nc.dram_tensor("out_t", (P, N), F32, kind="ExternalOutput").ap()
    build(nc, adj_tiles, x_t, weights, biases, out_t)
    result = run_bass_kernel_spmd(nc, [arrays], core_ids=[0])
    return np.ascontiguousarray(result.results[0]["out_t"].T)
```

```python
from contextlib import ExitStack

import numpy as np

import concourse.bass as bass
from concourse import mybir

F32 = mybir.dt.float32
F32R = mybir.dt.float32r
ACT = mybir.ActivationFunctionType
ALU = mybir.AluOpType

N = 4096
P = 128
BANK = 512
SEG = 1024
SEGS = N // SEG
TILES = N // P
SUB = SEG // P
PRODUCTS = 6
EPS = 1e-5
WEIGHTS = 7
BIASES = 4

WHOLE = [15, 31]
SPLIT = [j for j in range(TILES) if j not in WHOLE]
RAW_SLOTS = 6
SPLIT_SLOTS = 5
LOADS = len(SPLIT) // RAW_SLOTS
AHEAD = 5
assert len(SPLIT) % RAW_SLOTS == 0 and len(SPLIT) % SPLIT_SLOTS == 0
assert all((j + 1) % (2 * SUB) == 0 for j in WHOLE)

SUMMED = {0: (5, 9, 13, 15, 20, 25, 28, 31), 1: (0, 3, 7, 21, 29), 2: (2, 8, 10, 14, 19, 23),
          3: (), 4: (4, 6, 12, 17, 22, 27, 30), 5: (1, 11, 16, 18, 24, 26)}
SUM_ENDS = (2, 5)
assert sorted(sum(SUMMED.values(), ())) == list(range(TILES))

START = -1
NORMED = (START, 0, 2, 4)
PLAIN = (1, 3)

NORM = [("center", 5), ("square", 10), ("variance", 12), ("weight", 12), ("deviation", 17),
        ("inverse_deviation", 16), ("scale", 18), ("scale_rest", 18), ("split_high", 20),
        ("split_low", 21)]
WEIGHT_ONLY = [("evacuate", 4), ("weight", 6), ("split_high", 11), ("split_low", 12)]
STEPS = {
    0: [("evacuate", 4), ("residual", 5)] + NORM,
    1: WEIGHT_ONLY,
    2: [("evacuate", 4), ("residual", 5)] + NORM
       + [("diagonal", 24), ("broadcast", 28), ("normed", 31)],
    3: WEIGHT_ONLY,
    4: [("residual", 5)] + NORM,
    5: [("copy_degree", 2), ("divide", 5)],
}
START_STEPS = {
    1: [("deviation", 4), ("inverse_deviation", 3), ("scale", 4), ("scale_rest", 4),
        ("split_high", 5), ("split_low", 5)],
    2: [("center", 1), ("square", 6), ("variance", 6), ("weight", 6), ("deviation", 10),
        ("inverse_deviation", 10), ("scale", 11), ("scale_rest", 11), ("split_high", 12),
        ("split_low", 12)],
    3: [("center", 8), ("square", 13), ("variance", 13), ("weight", 13), ("deviation", 17),
        ("inverse_deviation", 17), ("scale", 18), ("scale_rest", 19), ("split_high", 20),
        ("split_low", 20)],
}
OWN_STEPS = {
    2: [("degree", 26), ("keep_degree", 30)],
    5: [("degree", 26), ("inverse_degree", 29), ("inverse_diagonal", 30),
        ("spread_degree", 30)],
}


def steps_after(p, q, j):
    first = isinstance(q, int)
    if p == 0 and first:
        steps = [(s, START, quarter) for quarter in START_STEPS
                 for s, at in START_STEPS[quarter] if at == j]
    else:
        kind, done = (p - 1, SEGS - 1) if first else (p, q - 1)
        steps = [(s, kind, done) for s, at in STEPS[kind] if at == j]
    return steps + [(s, p, q) for s, at in OWN_STEPS.get(p, []) if at == j]


def epilogues_before(kinds, kind):
    return SEGS * sum(k in kinds for k in range(START, kind))


def build(nc, adj_tiles, x_t, weights, biases, out_t):
    ctx = ExitStack()
    with ctx:
        def sbuf(name, shape, dtype=F32):
            return ctx.enter_context(nc.sbuf_tensor(name, shape, dtype))

        def psum(name, shape):
            return ctx.enter_context(nc.psum_tensor(name, shape, F32))

        def semaphore(name):
            return ctx.enter_context(nc.semaphore(name))

        g_high = [sbuf(f"g_high{i}", [P, N], F32R) for i in range(2)]
        g_low = [sbuf(f"g_low{i}", [P, N], F32R) for i in range(2)]
        g_whole = [sbuf(f"g_whole{i}", [P, len(WHOLE) * P]) for i in range(2)]
        x = sbuf("x", [P, N])
        h2 = sbuf("h2", [P, N])
        kept = sbuf("kept", [P, len(WHOLE), N])
        raw = sbuf("raw", [P, RAW_SLOTS, SEG])
        a_high = sbuf("a_high", [P, SPLIT_SLOTS, SEG], F32R)
        a_low = sbuf("a_low", [P, SPLIT_SLOTS, SEG], F32R)
        scratch = sbuf("scratch", [P, SEG])
        h = sbuf("h", [P, SEG])
        w = sbuf("w", [P, WEIGHTS, P])
        b = sbuf("b", [P, BIASES])
        identity = sbuf("identity", [P, P])
        centering = sbuf("centering", [P, P])
        ones = sbuf("ones", [P, P])
        average = sbuf("average", [P, 1])
        eps = sbuf("eps", [P, 1])
        std = sbuf("std", [P, SUB])
        rstd = sbuf("rstd", [P, SUB])
        degrees = sbuf("degrees", [P, SEGS * SUB])
        inverse = sbuf("inverse", [P, SUB])

        acc = psum("acc", [P, 2, SEG])
        centered = psum("centered", [P, SEG])
        g_psum = psum("g_psum", [P, SEG])

        raw_loaded = [semaphore(f"raw_loaded{i}") for i in range(RAW_SLOTS)]
        kept_loaded = [semaphore(f"kept_loaded{i}") for i in range(len(WHOLE))]
        x_loaded = [semaphore(f"x_loaded{i}") for i in range(SEGS)]
        small_loaded = semaphore("small_loaded")
        zeroed = semaphore("zeroed")
        identity_made = semaphore("identity_made")
        constants_made = semaphore("constants_made")
        weights_made = semaphore("weights_made")
        high_ready = semaphore("high_ready")
        low_ready = semaphore("low_ready")
        tile_added = semaphore("tile_added")
        tile_used = semaphore("tile_used")
        evacuated = semaphore("evacuated")
        x_ready = semaphore("x_ready")
        center_done = semaphore("center_done")
        square_ready = semaphore("square_ready")
        relu_ready = semaphore("relu_ready")
        variance_done = semaphore("variance_done")
        std_ready = semaphore("std_ready")
        rstd_ready = semaphore("rstd_ready")
        weight_done = semaphore("weight_done")
        scaled = semaphore("scaled")
        g_high_ready = semaphore("g_high_ready")
        g_whole_ready = semaphore("g_whole_ready")
        g_ready = semaphore("g_ready")
        diagonal_ready = semaphore("diagonal_ready")
        broadcast_done = semaphore("broadcast_done")
        h2_ready = semaphore("h2_ready")
        h2_used = semaphore("h2_used")
        degree_done = semaphore("degree_done")
        degree_kept = semaphore("degree_kept")
        degree_summed = semaphore("degree_summed")
        inverse_ready = semaphore("inverse_ready")
        inverse_diagonal_ready = semaphore("inverse_diagonal_ready")
        spread_done = semaphore("spread_done")
        spread_ready = semaphore("spread_ready")
        divided = semaphore("divided")
        out_ready = semaphore("out_ready")
        out_stored = semaphore("out_stored")

        W0, W1, W2, K0, K1, K2, W3 = (w[:, i, :] for i in range(7))
        TWICE_K2, K0_LESS_K2 = K2, K0
        WEIGHT = {START: W0, 0: W1, 1: W2, 2: TWICE_K2, 3: identity[:], 4: W3}

        def columns(tensor, q, first=0, size=SEG):
            return tensor[:, bass.ds(q * SEG + first, size)]

        def each_sub(ap):
            return ap.rearrange("p (s f) -> p s f", s=SUB)

        def tile_count(p, q, j):
            return (p * SEGS + q) * TILES + j + 1

        def split_count(p, q, j):
            return (p * SEGS + q) * len(SPLIT) + SPLIT.index(j % TILES) + 1 - (
                len(SPLIT) if j < 0 else 0)

        def added_count(p, q, j):
            if j < 0:
                owner = p - 1 if isinstance(q, int) else p
                return added_count(p, q, 0) - (0 in SUMMED[p]) - sum(
                    i > j + TILES for i in SUMMED[owner])
            before = SEGS * sum(len(SUMMED[i]) for i in range(p))
            return before + q * len(SUMMED[p]) + sum(i <= j for i in SUMMED[p])

        def raw_tile(j):
            return raw[:, SPLIT.index(j) % RAW_SLOTS, :]

        def whole_tile(q, j):
            return kept[:, WHOLE.index(j), bass.ds(q * SEG, SEG)]

        def wait_whole(engine, p, q, j):
            if p == 0:
                engine.wait_ge(kept_loaded[WHOLE.index(j)], 16 * (q + 1))

        def start_buffers(kind, q):
            if kind == START and q % 2:
                return acc[:, 1, :], h2[:, 2 * SEG:3 * SEG], h2[:, 3 * SEG:4 * SEG]
            return centered[:], scratch[:], h[:]

        def run_segments(engine, segment):
            for p in range(PRODUCTS):
                segment(p, 0)
                with engine.Fori(1, SEGS) as q:
                    segment(p, q)

        block = ctx.enter_context(nc.Block())

        @block.sync
        def _(sp):
            def segment(p, q):
                first = isinstance(q, int)
                for j in range(TILES):
                    source = adj_tiles[bass.ds(q * TILES + j, 1), :, :].rearrange("t p c -> (t p) c")
                    if j in WHOLE:
                        if p == 0:
                            sp.dma_start(whole_tile(q, j), source).then_inc(
                                kept_loaded[WHOLE.index(j)], 16)
                        continue
                    k = SPLIT.index(j)
                    if p or not first or k >= RAW_SLOTS:
                        before = SPLIT[k - RAW_SLOTS] - (TILES if k < RAW_SLOTS else 0)
                        owner = p - 1 if k < RAW_SLOTS and first else p
                        if before % TILES in SUMMED[owner]:
                            sp.wait_ge(tile_added, added_count(p, q, before))
                        else:
                            sp.wait_ge(low_ready, split_count(p, q, before))
                    sp.dma_start(raw_tile(j), source).then_inc(raw_loaded[k % RAW_SLOTS], 16)

            sp.dma_start(columns(x, 0), columns(x_t, 0)).then_inc(x_loaded[0], 16)
            run_segments(sp, segment)

        @block.gpsimd
        def _(pool):
            nc.gpsimd.memset(identity[:], 0.0).then_inc(zeroed, 1)
            pool.wait_ge(zeroed, 1)
            nc.gpsimd.affine_select(out=identity[:], in_=identity[:], compare_op=ALU.not_equal,
                                    fill=1.0, base=0, pattern=[[-1, P]],
                                    channel_multiplier=1).then_inc(identity_made, 1)
            with pool.Fori(0, SEGS) as q:
                pool.wait_ge(out_ready, q + 1)
                pool.dma_start(columns(out_t, q), columns(x, q)).then_inc(out_stored, 16)
                pool.wait_ge(out_stored, (q + 1) * 16)

        @block.scalar
        def _(act):
            act.dma_start(columns(x, 1), columns(x_t, 1)).then_inc(x_loaded[1], 16)
            act.dma_start(w[:], weights).then_inc(small_loaded, 16)
            act.dma_start(b[:], biases).then_inc(small_loaded, 16)
            for q in range(2, SEGS):
                act.dma_start(columns(x, q), columns(x_t, q)).then_inc(x_loaded[q], 16)
            act.wait_ge(constants_made, 1)
            nc.scalar.activation(std[:, 0:1], eps[:], ACT.Sqrt)

            def evacuate(kind, q):
                act.wait_ge(tile_used, tile_count(kind, q, TILES - 1))
                y = acc[:, q % 2, :]
                if kind == 3:
                    act.wait_ge(h2_ready, SEGS)
                    step = nc.scalar.activation(h[:], y, ACT.Copy)
                else:
                    bias = b[:, kind:kind + 1]
                    step = nc.scalar.activation(h[:] if kind == 1 else scratch[:], y, ACT.Relu, bias=bias)
                step.then_inc(evacuated, 1)

            def square(kind, q):
                e = epilogues_before(NORMED, kind) + q
                act.wait_ge(center_done, e + 1)
                source, squared, positive = start_buffers(kind, q)
                if kind == START and q == 2:
                    act.wait_ge(g_ready, q)
                nc.scalar.activation(squared, source, ACT.Square).then_inc(square_ready, 1)
                nc.scalar.activation(positive, source, ACT.Relu).then_inc(relu_ready, 1)

            def deviation(kind, q):
                e = epilogues_before(NORMED, kind) + q
                act.wait_ge(variance_done, e + 1)
                nc.scalar.activation(std[:], start_buffers(kind, q)[0][:, 0:SUB], ACT.Sqrt,
                                     bias=eps[:]).then_inc(std_ready, 1)

            def scale(kind, q, subs=range(SUB // 2)):
                act.wait_ge(weight_done, (kind + 1) * SEGS + q + 1)
                act.wait_ge(rstd_ready, epilogues_before(NORMED, kind) + q + 1)
                if kind == START and q:
                    act.wait_ge(g_ready, q)
                for s in subs:
                    nc.scalar.activation(each_sub(scratch[:])[:, s, :], each_sub(g_psum[:])[:, s, :],
                                         ACT.Copy, scale=rstd[:, s:s + 1]).then_inc(scaled, 1)

            def scale_rest(kind, q):
                scale(kind, q, range(SUB // 2, SUB))

            def split_high(kind, q):
                if kind in NORMED:
                    act.wait_ge(scaled, SUB * (epilogues_before(NORMED, kind) + q + 1))
                    source = scratch
                else:
                    act.wait_ge(weight_done, (kind + 1) * SEGS + q + 1)
                    source = g_psum
                nc.scalar.activation(g_whole[(kind + 1) % 2][:, bass.ds(q // 2 * P, P)],
                                     source[:, SEG - P:SEG], ACT.Copy).then_inc(g_whole_ready, 1)
                nc.scalar.activation(columns(g_high[(kind + 1) % 2], q), source[:],
                                     ACT.Copy).then_inc(g_high_ready, 1)

            def diagonals(out, column):
                for s in range(SUB):
                    step = nc.scalar.activation(each_sub(out)[:, s, :], identity[:], ACT.Copy,
                                                scale=column[:, s:s + 1])
                return step

            def diagonal(kind, q):
                diagonals(columns(h2, q), rstd).then_inc(diagonal_ready, 1)

            def inverse_diagonal(kind, q):
                act.wait_ge(inverse_ready, q + 1)
                diagonals(scratch[:], inverse).then_inc(inverse_diagonal_ready, 1)

            def copy_degree(kind, q):
                act.wait_ge(spread_done, q + 1)
                nc.scalar.activation(h[:], centered[:], ACT.Copy).then_inc(spread_ready, 1)

            steps = dict(evacuate=evacuate, square=square, deviation=deviation, scale=scale,
                         scale_rest=scale_rest, split_high=split_high,
                         diagonal=diagonal, inverse_diagonal=inverse_diagonal,
                         copy_degree=copy_degree)

            def split_tile(p, q, j):
                k = SPLIT.index(j)
                act.wait_ge(raw_loaded[k % RAW_SLOTS], 16 * ((p * SEGS + q) * LOADS + k // RAW_SLOTS + 1))
                if p or not isinstance(q, int) or k >= SPLIT_SLOTS:
                    before = SPLIT[k - SPLIT_SLOTS] - (TILES if k < SPLIT_SLOTS else 0)
                    act.wait_ge(tile_used, tile_count(p, q, before))
                nc.scalar.activation(a_high[:, k % SPLIT_SLOTS, :], raw_tile(j),
                                     ACT.Copy).then_inc(high_ready, 1)

            def segment(p, q):
                for j in range(TILES):
                    if j in SPLIT and (p or not isinstance(q, int) or j >= AHEAD):
                        split_tile(p, q, j)
                    for step, kind, done in steps_after(p, q, j):
                        if step in steps:
                            steps[step](kind, done)

            square(START, 0)
            for j in range(2):
                split_tile(0, 0, j)
            deviation(START, 0)
            square(START, 1)
            scale(START, 0)
            scale_rest(START, 0)
            split_high(START, 0)
            for j in range(2, AHEAD):
                split_tile(0, 0, j)
            act.wait_ge(weights_made, 2)
            run_segments(act, segment)
            copy_degree(PRODUCTS - 1, SEGS - 1)

        @block.vector
        def _(dve):
            nc.vector.memset(ones[:], 1.0)
            nc.vector.memset(average[:], 1.0 / P)
            nc.vector.memset(eps[:], EPS)
            dve.wait_ge(identity_made, 1)
            nc.vector.tensor_scalar(centering[:], identity[:], 1.0 / P, None,
                                    ALU.subtract).then_inc(constants_made, 1)
            dve.wait_ge(small_loaded, 32)
            nc.vector.tensor_tensor(K0_LESS_K2, K0, K2, ALU.subtract).then_inc(weights_made, 1)
            dve.wait_ge(weights_made, 1)
            nc.vector.tensor_scalar(TWICE_K2, K2, 2.0, None, ALU.mult).then_inc(weights_made, 1)

            def residual(kind, q):
                if kind == 4:
                    dve.wait_ge(tile_used, tile_count(kind, q, TILES - 1))
                    step = nc.vector.scalar_tensor_tensor(columns(x, q), acc[:, q % 2, :], b[:, 3:4],
                                                          columns(x, q), ALU.add, ALU.add)
                else:
                    dve.wait_ge(evacuated, kind * SEGS + q + 1)
                    step = nc.vector.tensor_tensor(columns(x, q), columns(x, q), scratch[:], ALU.add)
                step.then_inc(x_ready, 1)

            def inverse_deviation(kind, q):
                e = epilogues_before(NORMED, kind) + q
                dve.wait_ge(std_ready, e + 1)
                if kind == START and q:
                    dve.wait_ge(scaled, SUB * q)
                nc.vector.reciprocal(rstd[:], std[:]).then_inc(rstd_ready, 1)
                dve.wait_ge(rstd_ready, e + 1)

            def split_low(kind, q):
                dve.wait_ge(g_high_ready, (kind + 1) * SEGS + q + 1)
                source = scratch if kind in NORMED else g_psum
                nc.vector.tensor_tensor(columns(g_low[(kind + 1) % 2], q), source[:],
                                        columns(g_high[(kind + 1) % 2], q).bitcast(F32),
                                        ALU.subtract).then_inc(g_ready, 1)

            def normed(kind, q):
                dve.wait_ge(broadcast_done, q + 1)
                nc.vector.tensor_tensor(columns(h2, q), h[:], centered[:],
                                        ALU.mult).then_inc(h2_ready, 1)

            def keep_degree(p, q):
                dve.wait_ge(degree_done, SUM_ENDS.index(p) * SEGS + q + 1)
                nc.vector.tensor_copy(degrees[:, bass.ds(q * SUB, SUB)],
                                      g_psum[:, 0:SUB]).then_inc(degree_kept, 1)

            def inverse_degree(p, q):
                dve.wait_ge(degree_done, SUM_ENDS.index(p) * SEGS + q + 1)
                nc.vector.tensor_tensor(inverse[:], degrees[:, bass.ds(q * SUB, SUB)],
                                        centered[:, 0:SUB], ALU.add).then_inc(degree_summed, 1)
                dve.wait_ge(degree_summed, q + 1)
                nc.vector.reciprocal(inverse[:], inverse[:]).then_inc(inverse_ready, 1)

            def divide(p, q):
                dve.wait_ge(tile_used, tile_count(p, q, TILES - 1))
                dve.wait_ge(spread_ready, q + 1)
                nc.vector.tensor_tensor(scratch[:], acc[:, q % 2, :], h[:],
                                        ALU.mult).then_inc(divided, 1)
                dve.wait_ge(divided, q + 1)
                nc.vector.tensor_tensor(columns(x, q), columns(x, q), scratch[:],
                                        ALU.add).then_inc(out_ready, 1)

            def add_tile(p, q, j):
                mine = SUMMED[p]
                if j in WHOLE:
                    wait_whole(dve, p, q, j)
                tile = whole_tile(q, j) if j in WHOLE else raw_tile(j)
                sums = columns(h2, q)
                if p in (0, 4) and j == mine[0]:
                    if p == 4:
                        dve.wait_ge(h2_used, q + 1)
                    step = nc.vector.tensor_copy(sums, tile)
                else:
                    dve.wait_ge(tile_added, added_count(p, q, j) - 1)
                    out = sums
                    if p in SUM_ENDS and j == mine[-1]:
                        out = scratch[:]
                        if p < 5 or isinstance(q, int):
                            dve.wait_ge(g_ready, (p + 1) * SEGS + q)
                    step = nc.vector.tensor_tensor(out, sums, tile, ALU.add)
                step.then_inc(tile_added, 1)

            steps = dict(residual=residual, inverse_deviation=inverse_deviation, split_low=split_low,
                         normed=normed, keep_degree=keep_degree,
                         inverse_degree=inverse_degree, divide=divide)

            def split_tile(p, q, j):
                dve.wait_ge(high_ready, split_count(p, q, j))
                slot = SPLIT.index(j) % SPLIT_SLOTS
                nc.vector.tensor_tensor(a_low[:, slot, :], raw_tile(j), a_high[:, slot, :].bitcast(F32),
                                        ALU.subtract).then_inc(low_ready, 1)

            def segment(p, q):
                for j in range(TILES):
                    if j in SPLIT and (p or not isinstance(q, int) or j >= AHEAD):
                        split_tile(p, q, j)
                    if j in SUMMED[p]:
                        add_tile(p, q, j)
                    for step, kind, done in steps_after(p, q, j):
                        if step in steps:
                            steps[step](kind, done)

            for j in range(2):
                split_tile(0, 0, j)
            inverse_deviation(START, 0)
            split_low(START, 0)
            for j in range(2, AHEAD):
                split_tile(0, 0, j)
            run_segments(dve, segment)
            divide(PRODUCTS - 1, SEGS - 1)

        @block.tensor
        def _(pe):
            pe.wait_ge(constants_made, 1)

            def halves(out, lhsT, rhs, start=True, stop=True):
                for s in range(0, SEG, BANK):
                    last = nc.tensor.matmul(out[:, s:s + BANK], lhsT, rhs(s), start=start, stop=stop)
                return last

            def center(kind, q):
                e = epilogues_before(NORMED, kind) + q
                if kind > START or q > 1:
                    pe.wait_ge(std_ready, e if kind > START else q - 1)
                if kind == START:
                    pe.wait_ge(x_loaded[q], 16)
                else:
                    pe.wait_ge(x_ready, epilogues_before((0, 2, 4), kind) + q + 1)
                halves(start_buffers(kind, q)[0], centering[:],
                       lambda s: columns(x, q, s, BANK)).then_inc(center_done, 1)

            def variance(kind, q):
                e = epilogues_before(NORMED, kind) + q
                pe.wait_ge(square_ready, e + 1)
                pe.wait_ge(relu_ready, e + 1)
                out, squared, _ = start_buffers(kind, q)
                for s in range(SUB):
                    last = nc.tensor.matmul(out[:, s:s + 1], squared[:, s * P:s * P + P], average[:],
                                            start=True, stop=True)
                last.then_inc(variance_done, 1)

            def weight(kind, q):
                if kind in PLAIN:
                    pe.wait_ge(evacuated, kind * SEGS + q + 1)
                if kind == START and q:
                    pe.wait_ge(scaled, SUB * q)
                source = start_buffers(kind, q)[2]
                for s in range(SUB):
                    rows = g_psum[:, s * P:s * P + P]
                    if kind == 3:
                        last = nc.tensor.transpose(rows, source[:, s * P:s * P + P], identity[:])
                    else:
                        last = nc.tensor.matmul(rows, source[:, s * P:s * P + P], WEIGHT[kind],
                                                start=True, stop=True)
                last.then_inc(weight_done, 1)

            def broadcast(kind, q):
                pe.wait_ge(diagonal_ready, q + 1)
                halves(centered, ones[:], lambda s: columns(h2, q, s, BANK)).then_inc(broadcast_done, 1)

            def degree(p, q):
                pe.wait_ge(tile_added, added_count(p, q, SUMMED[p][-1]))
                if p == 5 and isinstance(q, int):
                    pe.wait_ge(std_ready, SEGS * len(NORMED))
                out = centered if p == 5 else g_psum
                for s in range(SUB):
                    last = nc.tensor.matmul(out[:, s:s + 1], scratch[:, s * P:s * P + P], ones[:, 0:1],
                                            start=True, stop=True)
                last.then_inc(degree_done, 1)

            def spread_degree(p, q):
                pe.wait_ge(inverse_diagonal_ready, q + 1)
                halves(centered, ones[:], lambda s: scratch[:, s:s + BANK]).then_inc(spread_done, 1)

            steps = dict(center=center, variance=variance, weight=weight, broadcast=broadcast,
                         degree=degree, spread_degree=spread_degree)

            def segment(p, q):
                first = isinstance(q, int)
                y = acc[:, q % 2, :]
                for j in range(TILES):
                    if first and j % SUB == 0:
                        pe.wait_ge(g_ready, p * SEGS + j // SUB + 1)
                    if j in WHOLE:
                        wait_whole(pe, p, q, j)
                        tile = whole_tile(q, j)
                        i = WHOLE.index(j)
                        step = halves(y, g_whole[p % 2][:, i * P:i * P + P],
                                      lambda s: tile[:, s:s + BANK],
                                      start=False, stop=j == TILES - 1)
                    else:
                        slot = SPLIT.index(j) % SPLIT_SLOTS
                        high = g_high[p % 2][:, j * P:j * P + P]
                        low = g_low[p % 2][:, j * P:j * P + P]
                        pe.wait_ge(low_ready, split_count(p, q, j))
                        for part, a, g in ((0, a_high, high), (1, a_low, high), (2, a_high, low)):
                            for s in range(0, SEG, BANK):
                                step = nc.tensor.matmul(y[:, s:s + BANK], g, a[:, slot, s:s + BANK],
                                                        start=j == 0 and part == 0, stop=False)
                    step.then_inc(tile_used, 1)
                    if p in (3, 4) and j == 0:
                        pe.wait_ge(h2_ready, q + 1)
                        step = halves(y, K1 if p == 3 else K0_LESS_K2,
                                      lambda s: columns(h2, q, s, BANK), start=False, stop=False)
                        if p == 4:
                            step.then_inc(h2_used, 1)
                    for step, kind, done in steps_after(p, q, j):
                        if step in steps:
                            steps[step](kind, done)

            center(START, 0)
            center(START, 1)
            variance(START, 0)
            pe.wait_ge(weights_made, 2)
            weight(START, 0)
            variance(START, 1)
            weight(START, 1)
            run_segments(pe, segment)


def kernel(x, adj, L0_gnn_kernel, L0_gnn_bias, L1_gnn_W1, L1_gnn_b1, L1_gnn_W2, L1_gnn_b2,
           L2_gnn_weight, L2_gnn_bias, L3_gnn_weight):
    import concourse.bacc as bacc
    from concourse.bass_utils import run_bass_kernel_spmd

    nc = bacc.Bacc("TRN2", target_bir_lowering=False, num_devices=1)
    arrays = {}

    def give(name, array):
        arrays[name] = np.ascontiguousarray(array)
        return nc.dram_tensor(name, arrays[name].shape, F32, kind="ExternalInput").ap()

    tiles = np.asarray(adj).reshape(SEGS, SEG, TILES, P).transpose(0, 2, 3, 1)
    adj_tiles = give("adj_tiles", tiles.reshape(SEGS * TILES, P, SEG))
    x_t = give("x_t", np.asarray(x).T)
    chebyshev = np.asarray(L2_gnn_weight)
    matrices = [L0_gnn_kernel, L1_gnn_W1, L1_gnn_W2, chebyshev[0], chebyshev[1], chebyshev[2],
                L3_gnn_weight]
    weights = give("weights", np.stack([np.asarray(m) for m in matrices], axis=1))
    vectors = [L0_gnn_bias, L1_gnn_b1, L1_gnn_b2, L2_gnn_bias]
    biases = give("biases", np.stack([np.asarray(v) for v in vectors], axis=1))
    out_t = nc.dram_tensor("out_t", (P, N), F32, kind="ExternalOutput").ap()
    build(nc, adj_tiles, x_t, weights, biases, out_t)
    result = run_bass_kernel_spmd(nc, [arrays], core_ids=[0])
    return np.ascontiguousarray(result.results[0]["out_t"].T)
```
